# Optimizing a Trainium2 kernel written in Bass

```python
import numpy as np
import jax
import jax.numpy as jnp

def _softmax(x, axis=-1):
    return jax.nn.softmax(x, axis=axis)

def _gelu(x):
    return jax.nn.gelu(x, approximate=True)

def _silu(x):
    return jax.nn.silu(x)

def _sigmoid(x):
    return jax.nn.sigmoid(x)

def _layernorm(x, axis=-1, eps=1e-05):
    m = jnp.mean(x, axis=axis, keepdims=True)
    v = jnp.var(x, axis=axis, keepdims=True)
    return (x - m) / jnp.sqrt(v + eps)

def _scatter_add(tgt, idx, src, axis=0):
    return tgt.at[idx].add(src)

def _segment_sum(src, seg, n):
    return jax.ops.segment_sum(src, seg, n)
kernel_name = 'mk_dlrm_tower_d1_rec_r8_9fbd2b'

def setup_inputs(seed: int=0):
    np.random.seed(seed)
    _w = jnp.asarray

    def _rec_inputs():
        import jax
        import jax.numpy as jnp
        _tk = jax.random.key(seed)
        ids = jnp.stack([jax.random.randint(jax.random.fold_in(_tk, 200 + f), (2048,), 0, v, jnp.int32) for f, v in enumerate([1250, 12500, 1000, 12500, 1250, 12500, 125000, 12500, 1250, 1250, 1250, 12500, 1000, 1250, 1250, 12500, 12500, 1000, 1000, 1000, 1000, 12500, 1250, 1250, 1000, 1000])], axis=1)
        tbl_0 = 0.05 * jax.random.normal(jax.random.fold_in(_tk, 500 + 0), (1250, 128), jnp.float32)
        tbl_1 = 0.05 * jax.random.normal(jax.random.fold_in(_tk, 500 + 1), (12500, 128), jnp.float32)
        tbl_2 = 0.05 * jax.random.normal(jax.random.fold_in(_tk, 500 + 2), (1000, 128), jnp.float32)
        tbl_3 = 0.05 * jax.random.normal(jax.random.fold_in(_tk, 500 + 3), (12500, 128), jnp.float32)
        tbl_4 = 0.05 * jax.random.normal(jax.random.fold_in(_tk, 500 + 4), (1250, 128), jnp.float32)
        tbl_5 = 0.05 * jax.random.normal(jax.random.fold_in(_tk, 500 + 5), (12500, 128), jnp.float32)
        tbl_6 = 0.05 * jax.random.normal(jax.random.fold_in(_tk, 500 + 6), (125000, 128), jnp.float32)
        tbl_7 = 0.05 * jax.random.normal(jax.random.fold_in(_tk, 500 + 7), (12500, 128), jnp.float32)
        tbl_8 = 0.05 * jax.random.normal(jax.random.fold_in(_tk, 500 + 8), (1250, 128), jnp.float32)
        tbl_9 = 0.05 * jax.random.normal(jax.random.fold_in(_tk, 500 + 9), (1250, 128), jnp.float32)
        tbl_10 = 0.05 * jax.random.normal(jax.random.fold_in(_tk, 500 + 10), (1250, 128), jnp.float32)
        tbl_11 = 0.05 * jax.random.normal(jax.random.fold_in(_tk, 500 + 11), (12500, 128), jnp.float32)
        tbl_12 = 0.05 * jax.random.normal(jax.random.fold_in(_tk, 500 + 12), (1000, 128), jnp.float32)
        tbl_13 = 0.05 * jax.random.normal(jax.random.fold_in(_tk, 500 + 13), (1250, 128), jnp.float32)
        tbl_14 = 0.05 * jax.random.normal(jax.random.fold_in(_tk, 500 + 14), (1250, 128), jnp.float32)
        tbl_15 = 0.05 * jax.random.normal(jax.random.fold_in(_tk, 500 + 15), (12500, 128), jnp.float32)
        tbl_16 = 0.05 * jax.random.normal(jax.random.fold_in(_tk, 500 + 16), (12500, 128), jnp.float32)
        tbl_17 = 0.05 * jax.random.normal(jax.random.fold_in(_tk, 500 + 17), (1000, 128), jnp.float32)
        tbl_18 = 0.05 * jax.random.normal(jax.random.fold_in(_tk, 500 + 18), (1000, 128), jnp.float32)
        tbl_19 = 0.05 * jax.random.normal(jax.random.fold_in(_tk, 500 + 19), (1000, 128), jnp.float32)
        tbl_20 = 0.05 * jax.random.normal(jax.random.fold_in(_tk, 500 + 20), (1000, 128), jnp.float32)
        tbl_21 = 0.05 * jax.random.normal(jax.random.fold_in(_tk, 500 + 21), (12500, 128), jnp.float32)
        tbl_22 = 0.05 * jax.random.normal(jax.random.fold_in(_tk, 500 + 22), (1250, 128), jnp.float32)
        tbl_23 = 0.05 * jax.random.normal(jax.random.fold_in(_tk, 500 + 23), (1250, 128), jnp.float32)
        tbl_24 = 0.05 * jax.random.normal(jax.random.fold_in(_tk, 500 + 24), (1000, 128), jnp.float32)
        tbl_25 = 0.05 * jax.random.normal(jax.random.fold_in(_tk, 500 + 25), (1000, 128), jnp.float32)
        _rk = jax.random.fold_in(_tk, 7)
        r_dense_features = -0.000520686 + 1.00062 * jax.random.normal(jax.random.fold_in(_rk, 101), (2048, 128), jnp.float32)
        W_top1 = 0.0405887 * jax.random.normal(jax.random.fold_in(_tk, 801), (607, 512), jnp.float32)
        W_top2 = 0.0441942 * jax.random.normal(jax.random.fold_in(_tk, 802), (512, 256), jnp.float32)
        W_top3 = 0.0625 * jax.random.normal(jax.random.fold_in(_tk, 803), (256, 1), jnp.float32)
        b_top1 = jnp.zeros((512,), jnp.float32)
        b_top2 = jnp.zeros((256,), jnp.float32)
        return (r_dense_features, ids, tbl_0, tbl_1, tbl_2, tbl_3, tbl_4, tbl_5, tbl_6, tbl_7, tbl_8, tbl_9, tbl_10, tbl_11, tbl_12, tbl_13, tbl_14, tbl_15, tbl_16, tbl_17, tbl_18, tbl_19, tbl_20, tbl_21, tbl_22, tbl_23, tbl_24, tbl_25, W_top1, b_top1, W_top2, b_top2, W_top3)
    r_dense_features, ids, tbl_0, tbl_1, tbl_2, tbl_3, tbl_4, tbl_5, tbl_6, tbl_7, tbl_8, tbl_9, tbl_10, tbl_11, tbl_12, tbl_13, tbl_14, tbl_15, tbl_16, tbl_17, tbl_18, tbl_19, tbl_20, tbl_21, tbl_22, tbl_23, tbl_24, tbl_25, W_top1, b_top1, W_top2, b_top2, W_top3 = _rec_inputs()

    def _L0_rec_setup():
        import jax, jax.numpy as jnp
        import numpy as np
        B, F, D = (2048, 26, 128)
        key = jax.random.key(seed)
        k1, k2 = jax.random.split(key)
        dense_features = jax.random.normal(k1, (B, D), dtype=jnp.float32)
        sparse_values = jax.random.normal(k2, (B, F, D), dtype=jnp.float32)
        return {'dense_features': dense_features, 'sparse_values': sparse_values}
    _L0_rec_all = _L0_rec_setup()
    _L0_rec_in = {k: v for k, v in _L0_rec_all.items() if k in ()}
    del _L0_rec_all
    return {'r_dense_features': r_dense_features, 'ids': ids, 'tbl_0': tbl_0, 'tbl_1': tbl_1, 'tbl_2': tbl_2, 'tbl_3': tbl_3, 'tbl_4': tbl_4, 'tbl_5': tbl_5, 'tbl_6': tbl_6, 'tbl_7': tbl_7, 'tbl_8': tbl_8, 'tbl_9': tbl_9, 'tbl_10': tbl_10, 'tbl_11': tbl_11, 'tbl_12': tbl_12, 'tbl_13': tbl_13, 'tbl_14': tbl_14, 'tbl_15': tbl_15, 'tbl_16': tbl_16, 'tbl_17': tbl_17, 'tbl_18': tbl_18, 'tbl_19': tbl_19, 'tbl_20': tbl_20, 'tbl_21': tbl_21, 'tbl_22': tbl_22, 'tbl_23': tbl_23, 'tbl_24': tbl_24, 'tbl_25': tbl_25, 'W_top1': W_top1, 'b_top1': b_top1, 'W_top2': W_top2, 'b_top2': b_top2, 'W_top3': W_top3}

def reference(r_dense_features, ids, tbl_0, tbl_1, tbl_2, tbl_3, tbl_4, tbl_5, tbl_6, tbl_7, tbl_8, tbl_9, tbl_10, tbl_11, tbl_12, tbl_13, tbl_14, tbl_15, tbl_16, tbl_17, tbl_18, tbl_19, tbl_20, tbl_21, tbl_22, tbl_23, tbl_24, tbl_25, W_top1, b_top1, W_top2, b_top2, W_top3):
    import jax
    import jax.numpy as jnp

    def _L0_rec_ref(dense_features, sparse_values):
        import jax, jax.numpy as jnp
        import numpy as np
        B, F, D = (2048, 26, 128)
        sd = jnp.einsum('bfd,bd->bf', sparse_values, dense_features)
        ss = jnp.einsum('bfd,bgd->bfg', sparse_values, sparse_values)
        iu, ju = jnp.triu_indices(F, k=1)
        pairs = ss[:, iu, ju]
        return jnp.concatenate([dense_features, sd, pairs], axis=1)
    e = jnp.stack([tbl_0[ids[:, 0]], tbl_1[ids[:, 1]], tbl_2[ids[:, 2]], tbl_3[ids[:, 3]], tbl_4[ids[:, 4]], tbl_5[ids[:, 5]], tbl_6[ids[:, 6]], tbl_7[ids[:, 7]], tbl_8[ids[:, 8]], tbl_9[ids[:, 9]], tbl_10[ids[:, 10]], tbl_11[ids[:, 11]], tbl_12[ids[:, 12]], tbl_13[ids[:, 13]], tbl_14[ids[:, 14]], tbl_15[ids[:, 15]], tbl_16[ids[:, 16]], tbl_17[ids[:, 17]], tbl_18[ids[:, 18]], tbl_19[ids[:, 19]], tbl_20[ids[:, 20]], tbl_21[ids[:, 21]], tbl_22[ids[:, 22]], tbl_23[ids[:, 23]], tbl_24[ids[:, 24]], tbl_25[ids[:, 25]]], axis=1)
    z = _L0_rec_ref(r_dense_features, e)
    z = z.reshape(z.shape[0], -1)
    h = jnp.concatenate([z, r_dense_features], axis=1)
    h = jnp.maximum(h @ W_top1 + b_top1, 0.0)
    h = jnp.maximum(h @ W_top2 + b_top2, 0.0)
    y = h @ W_top3
    return y

_drawn_inputs = setup_inputs


def setup_inputs(seed=0):
    import zlib

    import numpy as np

    out = dict(_drawn_inputs(seed))
    spreads = {'b_top1': (0.0, 0.1), 'b_top2': (0.0, 0.1)}
    factors = {}
    for name, (base, spread) in spreads.items():
        noise = np.random.default_rng([zlib.crc32(name.encode()), seed]).standard_normal(out[name].shape)
        drawn = base * np.exp(spread * noise) if base else spread * noise
        out[name] = jnp.asarray(drawn.astype(out[name].dtype))
    for name, factor in factors.items():
        out[name] = (out[name] * factor).astype(out[name].dtype)
    return out
```

```python
from contextlib import ExitStack

import concourse.bass as bass
import numpy as np
from concourse import mybir

ALU = mybir.AluOpType
ACT = mybir.ActivationFunctionType
F32 = mybir.dt.float32
F32R = mybir.dt.float32r
I32 = mybir.dt.int32

B, F, D = 2048, 26, 128
H1, H2 = 512, 256
NF = F + 1
TILE = 128
PAIR = 2 * TILE
NT, NP, NB = B // TILE, B // PAIR, B // (4 * TILE)

ONE_HOT = (2, 12, 17, 18, 19, 20, 24)
GATHERED = tuple(f for f in range(F) if f not in ONE_HOT)
NO, NG = len(ONE_HOT), len(GATHERED)
OH_ROWS = 1000
OH_CHUNKS = 8
OH_K = OH_ROWS // OH_CHUNKS
SET = 4 * TILE
N_STAGED = 4
ORDER = GATHERED + ONE_HOT + (F,)

HALF = NF // 2
NSLOT = HALF + 1
LABEL = [(-s) % NF for s in range(NSLOT)] + [(HALF - s) % NF for s in range(NSLOT - 1)]
QUAD = 32
SPQ = 4
KCH = SPQ


def slot_source(row, slot):
    for over, position in ((False, slot), (True, NSLOT + slot)):
        if position < NF and 1 <= (LABEL[position] - LABEL[row]) % NF <= HALF:
            return position, over
    return None, False


def top1_row(a, b):
    a, b = min(a, b), max(a, b)
    if b == F:
        return D + a
    return D + F + a * F - a * (a + 1) // 2 + (b - a - 1)


def build(nc, ids, one_hot_ids, x_t, tables, w1_pairs, w_top1, b1_cols, w_top2, b2_cols, w3_cols,
          row_numbers, over_mask, identity, out):
    with ExitStack() as ctx:
        def sb(name, shape, dt, stack=ctx):
            return stack.enter_context(nc.sbuf_tensor(name, shape, dt))

        def sem(name):
            return ctx.enter_context(nc.semaphore(name))

        index_all = sb("index_all", [128, NT, F], I32)
        index_now = sb("index_now", [128, 4, F], I32)
        gathered = sb("gathered", [128, 4, NG, D], F32)
        fixed = sb("fixed", [128, NO, SET], F32)
        dense_t = sb("dense_t", [128, B], F32)
        high = [sb(f"high{k}", [OH_K, OH_CHUNKS, D], F32R) for k in range(NO)]
        low = [sb(f"low{k}", [OH_K, OH_CHUNKS, D], F32R) for k in range(NO)]
        ids_row = sb("ids_row", [128, NO, SET], I32)
        onehot = [sb(f"onehot{i}", [OH_K, SET], F32R) for i in range(4)]
        embed = [sb(f"embed{i}", [128, TILE, NF], F32) for i in range(2)]
        w1p = sb("w1p", [128, KCH, H1], F32)
        w1d = sb("w1d", [128, H1], F32)
        w2 = sb("w2", [128, H1 // 128, H2], F32)
        w3 = sb("w3", [128, H2 // 128], F32)
        b1 = sb("b1", [128, H1 // 128], F32)
        b2 = sb("b2", [128, H2 // 128], F32)
        row_no = sb("row_no", [128, OH_CHUNKS], F32)
        mask = sb("mask", [128, NSLOT - 1], I32)
        ident = sb("ident", [128, 128], F32)

        with ExitStack() as preparation:
            table = [sb(f"table{i}", [OH_K, OH_CHUNKS, D], F32, preparation) for i in range(N_STAGED)]
            w1d_last = sb("w1d_last", [128, H1], F32, preparation)

        slots = [sb(f"slots{i}", [128, NSLOT, 64], F32) for i in range(2)]
        zpairs = [sb(f"zpairs{i}", [128, KCH, PAIR], F32) for i in range(2)]
        h1 = sb("h1", [128, H1 // 128, PAIR], F32)
        h2 = sb("h2", [128, H2 // 128, PAIR], F32)

        turned = [ctx.enter_context(nc.psum_tensor(f"turned{i}", [128, 4, 128], F32)) for i in range(2)]
        gram = [ctx.enter_context(nc.psum_tensor(f"gram{i}", [128, 512], F32)) for i in range(2)]
        acc = ctx.enter_context(nc.psum_tensor("acc", [128, 4, 512], F32))

        index_loaded = sem("index_loaded")
        row_numbers_loaded = sem("row_numbers_loaded")
        consts_loaded = sem("consts_loaded")
        weights_loaded = sem("weights_loaded")
        dense_loaded = sem("dense_loaded")
        first_ids_loaded = [sem(f"first_ids_loaded{k}") for k in range(NO)]
        ids_loaded = sem("ids_loaded")
        table_loaded = [sem(f"table_loaded{i}") for i in range(N_STAGED)]
        high_ready = sem("high_ready")
        low_ready = sem("low_ready")
        onehot_ready = sem("onehot_ready")
        onehot_used = sem("onehot_used")
        lookup_ready = sem("lookup_ready")
        lookup_kept = sem("lookup_kept")
        index_ready = sem("index_ready")
        rows_landed = [sem(f"rows_landed{i}") for i in range(4)]
        turned_ready = [sem(f"turned_ready{i}") for i in range(2)]
        turned_kept = [sem(f"turned_kept{i}") for i in range(2)]
        fixed_placed = sem("fixed_placed")
        gram_ready = sem("gram_ready")
        slots_copied = sem("slots_copied")
        slots_ready = sem("slots_ready")
        w1d_summed = sem("w1d_summed")
        moved_act = sem("moved_act")
        moved_dve = sem("moved_dve")
        act_in = sem("act_in")
        act_out = sem("act_out")
        dve_in = sem("dve_in")
        dve_out = sem("dve_out")
        y_stored = sem("y_stored")

        N_CONSTS, N_WEIGHTS = 2, 7

        block = ctx.enter_context(nc.Block())

        GROUPS = [range(g, min(g + 4, NG)) for g in range(0, NG, 4)]
        NGR = len(GROUPS)
        assert NGR % 2 == 1

        def groups_before(t, m, g, parity):
            return (2 * NGR) * t + (NGR * m + g + (1 - parity)) // 2

        USED = OH_CHUNKS - 1

        MOVED_BY_ACT = (3, 2)

        def due(value):
            return not isinstance(value, int) or value > 0

        @block.sync
        def _(sp):
            sp.dma_start(index_all[:], ids.rearrange("(n p) f -> p n f", p=128)).then_inc(index_loaded, 16)
            sp.dma_start(row_no[:], row_numbers).then_inc(row_numbers_loaded, 16)
            for k in range(NO):
                sp.dma_start(ids_row[:, k, :], one_hot_ids[:, k, 0:SET].to_broadcast([128, SET])
                             ).then_inc(first_ids_loaded[k], 16)
                if k >= N_STAGED:
                    sp.wait_ge(low_ready, k - N_STAGED + 1)
                sp.dma_start(table[k % N_STAGED][:], tables[ONE_HOT[k]].rearrange("(p c) d -> p c d", c=OH_CHUNKS)
                             ).then_inc(table_loaded[k % N_STAGED], 16)
            sp.dma_start(ident[:], identity).then_inc(consts_loaded, 16)
            sp.dma_start(mask[:], over_mask).then_inc(consts_loaded, 16)
            sp.dma_start(dense_t[:], x_t).then_inc(dense_loaded, 16)
            sp.dma_start(w1d[:], w_top1[0:D, :]).then_inc(weights_loaded, 16)
            sp.dma_start(w1d_last[:], w_top1[w_top1.shape[0] - D:w_top1.shape[0], :]).then_inc(weights_loaded, 16)
            sp.dma_start(b1[:], b1_cols).then_inc(weights_loaded, 16)
            sp.dma_start(w1p[:], w1_pairs.rearrange("c p h -> p c h")).then_inc(weights_loaded, 16)
            sp.dma_start(w2[:], w_top2.rearrange("(k p) h -> p k h", p=128)).then_inc(weights_loaded, 16)
            sp.dma_start(b2[:], b2_cols).then_inc(weights_loaded, 16)
            sp.dma_start(w3[:], w3_cols).then_inc(weights_loaded, 16)

            sp.wait_ge(act_out, 4 * NP)
            sp.dma_start(out, dense_t[0:1, :]).then_inc(y_stored, 16)
            sp.wait_ge(y_stored, 16)

        @block.gpsimd
        def _(pool):
            pool.wait_ge(index_loaded, 16)

            def copy_index(t, m):
                nc.gpsimd.tensor_copy(index_now[:, m, :], index_all[:, 4 * t + m, :]).then_inc(index_ready, 1)

            def gather(t, m, last=False):
                pool.wait_ge(index_ready, 4 * t + m + 1)
                end = (NGR * m + NGR - 1) % 2
                if due(groups_before(t - 1, m, NGR, end)):
                    pool.wait_ge(turned_ready[end], groups_before(t - 1, m, NGR, end))
                tn, mn = (t, m + 1) if m < 3 else (t + 1, 0)
                if due(16 * NG * tn):
                    pool.wait_ge(rows_landed[mn], 16 * NG * tn)
                if not last:
                    copy_index(tn, mn)
                for g, f in enumerate(GATHERED):
                    nc.gpsimd.indirect_dma_start(
                        gathered[:, m, g, :], None, tables[f],
                        bass.IndirectOffsetOnAxis(ap=index_now[:, m, f:f + 1], axis=0),
                    ).then_inc(rows_landed[m], 16)

            copy_index(0, 0)
            for m in range(4):
                gather(0, m)
            with pool.Fori(1, NB - 1) as t:
                for m in range(4):
                    gather(t, m)
            for m in range(4):
                gather(NB - 1, m, last=(m == 3))

        @block.tensor
        def _(pe):
            def look_up(t, k):
                q = NO * t + k
                if k >= 2:
                    pe.wait_ge(lookup_kept, q - 1)
                if isinstance(t, int) and t == 0:
                    pe.wait_ge(high_ready, k + 1)
                    pe.wait_ge(low_ready, k + 1)
                for c in range(OH_CHUNKS):
                    pe.wait_ge(onehot_ready, OH_CHUNKS * q + c + 1)
                    nc.tensor.matmul(acc[:, k % 2, :], high[k][:, c, :], onehot[c % 4][:],
                                     start=(c == 0), stop=False)
                    nc.tensor.matmul(acc[:, k % 2, :], low[k][:, c, :], onehot[c % 4][:],
                                     start=False, stop=(c == USED)
                                     ).then_inc(onehot_used if c < USED else lookup_ready, 1)

            def transpose_rows(t, m, groups=range(NGR)):
                for g in groups:
                    if g == 0:
                        pe.wait_ge(rows_landed[m], 16 * NG * (t + 1))
                    parity = (NGR * m + g) % 2
                    if due(groups_before(t, m, g, parity)):
                        pe.wait_ge(turned_kept[parity], groups_before(t, m, g, parity))
                    for n, r in enumerate(GROUPS[g]):
                        mm = nc.tensor.transpose(turned[parity][:, n, :], gathered[:, m, r, :], ident[:])
                    mm.then_inc(turned_ready[parity], 1)

            def gram_half(t, m, b, turning=None):
                if b == 0:
                    pe.wait_ge(fixed_placed, 4 * t + m + 1)
                    pe.wait_ge(turned_kept[0], groups_before(t, m, NGR, 0))
                    pe.wait_ge(turned_kept[1], groups_before(t, m, NGR, 1))
                if due(8 * t + 2 * m + b - 1):
                    pe.wait_ge(slots_ready, 8 * t + 2 * m + b - 1)
                for i in range(16):
                    if turning and i % 2 == 0 and i // 2 - 1 in range(NGR):
                        transpose_rows(*turning, groups=[i // 2 - 1])
                    for j in range(4):
                        rows = embed[m % 2][:, 32 * j + 16 * b + i, :]
                        mm = nc.tensor.matmul(gram[b][QUAD * j:QUAD * j + NF, NF * i:NF * (i + 1)],
                                              rows, rows, start=True, stop=True)
                mm.then_inc(gram_ready, 1)

            def tower(t, a, last=False):
                u = 2 * t + a
                dense = dense_t[:, bass.ds(PAIR * u, PAIR)].rearrange("p (n j i) -> p j n i", n=2, j=4)
                for c in range(4):
                    if c == 0 and a == 0 and not last:
                        pe.wait_ge(lookup_kept, NO * (t + 2))
                    if c == 2:
                        pe.wait_ge(act_out, 4 * u + 1)
                    if c == 3:
                        pe.wait_ge(dve_out, 3 * u + 1)
                    cols = slice(128 * c, 128 * (c + 1))
                    nc.tensor.matmul(acc[:, c % 2, 0:PAIR], w1d[:, cols], dense, start=True, stop=False)
                    if c == 0:
                        pe.wait_ge(moved_act, u + 1)
                        pe.wait_ge(moved_dve, u + 1)
                    for s in range(KCH):
                        k = QUAD * sum(SPQ * q + s < NSLOT for q in range(4))
                        mm = nc.tensor.matmul(acc[:, c % 2, 0:PAIR], w1p[0:k, s, cols], zpairs[a][0:k, s, :],
                                              start=False, stop=(s == KCH - 1))
                    mm.then_inc(act_in if c % 2 == 0 else dve_in, 1)
                for c in range(4):
                    if c % 2 == 0:
                        pe.wait_ge(act_out, 4 * u + 1 + c // 2)
                    else:
                        pe.wait_ge(dve_out, 3 * u + 1 + c // 2)
                    for o in range(2):
                        mm = nc.tensor.matmul(acc[:, 2 + o, 0:PAIR], w2[:, c, 128 * o:128 * (o + 1)], h1[:, c, :],
                                              start=(c == 0), stop=(c == 3))
                        if c == 3:
                            mm.then_inc(act_in if o == 0 else dve_in, 1)
                pe.wait_ge(act_out, 4 * u + 3)
                nc.tensor.matmul(acc[0:1, 2, 0:PAIR], w3[:, 0:1], h2[:, 0, :], start=True, stop=False)
                pe.wait_ge(dve_out, 3 * u + 3)
                nc.tensor.matmul(acc[0:1, 2, 0:PAIR], w3[:, 1:2], h2[:, 1, :], start=False, stop=True
                                 ).then_inc(act_in, 1)

            def four_tiles(t, first=False, last=False):
                gram_half(t, 0, 0)
                if not first:
                    tower(t - 1, 1)
                gram_half(t, 0, 1, turning=(t, 1))
                gram_half(t, 1, 0)
                gram_half(t, 1, 1, turning=None if first else (t, 2))
                if not last:
                    for k in range(NO):
                        look_up(t + 1, k)
                        if first and k == NO // 2:
                            transpose_rows(t, 2)
                gram_half(t, 2, 0)
                if last:
                    tower(t, 0, last)
                gram_half(t, 2, 1, turning=(t, 3))
                if first:
                    pe.wait_ge(weights_loaded, 16 * N_WEIGHTS)
                    pe.wait_ge(w1d_summed, 1)
                if not last:
                    tower(t, 0)
                gram_half(t, 3, 0)
                gram_half(t, 3, 1, turning=None if last else (t + 1, 0))
                if last:
                    tower(t, 1)

            for k in range(NO):
                if k == NO - 1:
                    pe.wait_ge(consts_loaded, 16 * N_CONSTS)
                    transpose_rows(0, 0)
                look_up(0, k)
            four_tiles(0, first=True)
            with pe.Fori(1, NB - 1) as t:
                four_tiles(t)
            four_tiles(NB - 1, last=True)

        @block.scalar
        def _(act):
            def split_high(k):
                act.wait_ge(table_loaded[k % N_STAGED], 16 * (k // N_STAGED + 1))
                nc.scalar.copy(high[k][:], table[k % N_STAGED][:]).then_inc(high_ready, 1)

            def keep_lookup(t, k):
                act.wait_ge(lookup_ready, NO * t + k + 1)
                nc.scalar.copy(fixed[:, k, :], acc[:, k % 2, :]).then_inc(lookup_kept, 1)

            def load_ids(t):
                act.dma_start(ids_row[:], one_hot_ids[:, :, bass.ds(SET * t, SET)].to_broadcast([128, NO, SET])
                              ).then_inc(ids_loaded, 16)

            def keep_turned(t, m):
                if due(8 * t + 2 * m - 2):
                    act.wait_ge(gram_ready, 8 * t + 2 * m - 2)
                for g, group in enumerate(GROUPS):
                    if (NGR * m + g) % 2 == 0:
                        act.wait_ge(turned_ready[0], groups_before(t, m, g, 0) + 1)
                        nc.scalar.copy(embed[m % 2][:, :, group[0]:group[-1] + 1].rearrange("p n f -> p f n"),
                                       turned[0][:, 0:len(group), :]).then_inc(turned_kept[0], 1)

            def place_fixed(t, m):
                if due(8 * t + 2 * m - 2):
                    act.wait_ge(gram_ready, 8 * t + 2 * m - 2)
                nc.scalar.copy(embed[m % 2][:, :, NG:F].rearrange("p n f -> p f n"),
                               fixed[:, :, TILE * m:TILE * (m + 1)])
                nc.scalar.copy(embed[m % 2][:, :, F], dense_t[:, bass.ds(TILE * (4 * t + m), TILE)]
                               ).then_inc(fixed_placed, 1)

            def copy_slots(t, m, b):
                if m % 2 == 0 and b == 0 and due(2 * t + m // 2 - 1):
                    act.wait_ge(moved_dve, 2 * t + m // 2 - 1)
                act.wait_ge(gram_ready, 8 * t + 2 * m + b + 1)
                i0 = 32 * (m % 2) + 16 * b
                nc.scalar.copy(slots[m // 2][:, 0:NSLOT - 1, i0:i0 + 16],
                               gram[b][:, 0:16 * NF].rearrange("p (i f) -> p f i", f=NF)[:, 0:NSLOT - 1, :]
                               ).then_inc(slots_copied, 1)

            def move_slots(t, a):
                act.wait_ge(slots_ready, 8 * t + 4 * (a + 1))
                for j in range(MOVED_BY_ACT[a]):
                    for q in range(4):
                        n = min(SPQ, NSLOT - SPQ * q)
                        ins = nc.scalar.copy(zpairs[a][QUAD * q:QUAD * (q + 1), 0:n, 64 * j:64 * (j + 1)],
                                             slots[a][QUAD * j:QUAD * (j + 1), SPQ * q:SPQ * q + n, :])
                ins.then_inc(moved_act, 1)

            def tower(t, a):
                u = 2 * t + a
                for n, c in enumerate((0, 2)):
                    act.wait_ge(act_in, 4 * u + n + 1)
                    nc.scalar.activation(h1[:, c, :], acc[:, 0, 0:PAIR], ACT.Relu, bias=b1[:, c:c + 1]
                                         ).then_inc(act_out, 1)
                act.wait_ge(act_in, 4 * u + 3)
                nc.scalar.activation(h2[:, 0, :], acc[:, 2, 0:PAIR], ACT.Relu, bias=b2[:, 0:1]).then_inc(act_out, 1)
                act.wait_ge(act_in, 4 * u + 4)
                for n in range(2):
                    ins = nc.scalar.copy(dense_t[0:1, bass.ds(PAIR * u + TILE * n, TILE)].rearrange("p (j i) -> p j i", j=4),
                                         acc[0:1, 2, 0:PAIR].rearrange("p (j n i) -> p n j i", n=2, j=4)[:, n])
                ins.then_inc(act_out, 1)

            def four_tiles(t, first=False, last=False):
                if not last:
                    load_ids(t + 1)
                copy_slots(t, 0, 0)
                place_fixed(t, 1)
                if not first:
                    tower(t - 1, 1)
                keep_turned(t, 1)
                copy_slots(t, 0, 1)
                copy_slots(t, 1, 0)
                place_fixed(t, 2)
                if not first:
                    keep_turned(t, 2)
                copy_slots(t, 1, 1)
                place_fixed(t, 3)
                if not last:
                    act.wait_ge(fixed_placed, 4 * t + 4)
                    for k in range(NO):
                        keep_lookup(t + 1, k)
                        if k == 0:
                            move_slots(t, 0)
                        if first and k == NO // 2:
                            keep_turned(t, 2)
                else:
                    move_slots(t, 0)
                copy_slots(t, 2, 0)
                if last:
                    tower(t, 0)
                keep_turned(t, 3)
                copy_slots(t, 2, 1)
                if not last:
                    tower(t, 0)
                copy_slots(t, 3, 0)
                if not last:
                    act.wait_ge(lookup_kept, NO * (t + 2))
                    place_fixed(t + 1, 0)
                    keep_turned(t + 1, 0)
                copy_slots(t, 3, 1)
                move_slots(t, 1)
                if last:
                    tower(t, 1)

            split_high(0)
            split_high(1)
            for k in range(NO):
                if k + 2 < NO:
                    split_high(k + 2)
                if k == NO - 1:
                    keep_turned(0, 0)
                keep_lookup(0, k)
            act.wait_ge(dense_loaded, 16)
            act.wait_ge(weights_loaded, 16 * N_WEIGHTS)
            act.wait_ge(lookup_kept, NO)
            place_fixed(0, 0)
            four_tiles(0, first=True)
            with act.Fori(1, NB - 1) as t:
                four_tiles(t)
            four_tiles(NB - 1, last=True)

        @block.vector
        def _(dve):
            for b in range(2):
                nc.vector.memset(gram[b][:], 0.0)

            def split_low(k):
                dve.wait_ge(table_loaded[k % N_STAGED], 16 * (k // N_STAGED + 1))
                dve.wait_ge(high_ready, k + 1)
                nc.vector.tensor_tensor(low[k][:], table[k % N_STAGED][:], high[k][:].bitcast(F32), ALU.subtract
                                        ).then_inc(low_ready, 1)

            def one_hots(t, k, chunks=range(OH_CHUNKS)):
                q = NO * t + k
                for c in chunks:
                    if c == 0:
                        if isinstance(t, int) and t == 0:
                            dve.wait_ge(first_ids_loaded[k], 16)
                        else:
                            dve.wait_ge(ids_loaded, 16 * t)
                    if c >= 4:
                        dve.wait_ge(onehot_used, USED * q + c - 3)
                    elif due(q):
                        if c == 3:
                            dve.wait_ge(lookup_ready, q)
                        else:
                            dve.wait_ge(onehot_used, USED * (q - 1) + c + 5)
                    nc.vector.tensor_scalar(onehot[c % 4][:], ids_row[0:OH_K, k, :],
                                            row_no[0:OH_K, c:c + 1], None, ALU.is_equal
                                            ).then_inc(onehot_ready, 1)

            def keep_turned(t, m):
                if due(8 * t + 2 * m - 2):
                    dve.wait_ge(gram_ready, 8 * t + 2 * m - 2)
                for g, group in enumerate(GROUPS):
                    if (NGR * m + g) % 2 == 1:
                        dve.wait_ge(turned_ready[1], groups_before(t, m, g, 1) + 1)
                        nc.vector.tensor_copy(embed[m % 2][:, :, group[0]:group[-1] + 1].rearrange("p n f -> p f n"),
                                              turned[1][:, 0:len(group), :]).then_inc(turned_kept[1], 1)

            def lay_over(t, m, b):
                dve.wait_ge(slots_copied, 8 * t + 2 * m + b + 1)
                i0 = 32 * (m % 2) + 16 * b
                columns = gram[b][:, 0:16 * NF].rearrange("p (i f) -> p f i", f=NF)
                nc.vector.tensor_copy(slots[m // 2][:, NSLOT - 1, i0:i0 + 16], columns[:, NSLOT - 1, :])
                nc.vector.copy_predicated(
                    slots[m // 2][:, 0:NSLOT - 1, i0:i0 + 16],
                    mask[:].unsqueeze(2).to_broadcast([128, NSLOT - 1, 16]), columns[:, NSLOT:NF, :]
                ).then_inc(slots_ready, 1)

            def move_slots(t, a):
                dve.wait_ge(slots_ready, 8 * t + 4 * (a + 1))
                for j in range(MOVED_BY_ACT[a], 4):
                    for q in range(4):
                        n = min(SPQ, NSLOT - SPQ * q)
                        ins = nc.vector.tensor_copy(zpairs[a][QUAD * q:QUAD * (q + 1), 0:n, 64 * j:64 * (j + 1)],
                                                    slots[a][QUAD * j:QUAD * (j + 1), SPQ * q:SPQ * q + n, :])
                ins.then_inc(moved_dve, 1)

            def tower(t, a):
                u = 2 * t + a
                for n, c in enumerate((1, 3)):
                    dve.wait_ge(dve_in, 3 * u + n + 1)
                    nc.vector.tensor_scalar(h1[:, c, :], acc[:, 1, 0:PAIR], b1[:, c:c + 1], 0.0, ALU.add, ALU.max
                                            ).then_inc(dve_out, 1)
                dve.wait_ge(dve_in, 3 * u + 3)
                nc.vector.tensor_scalar(h2[:, 1, :], acc[:, 3, 0:PAIR], b2[:, 1:2], 0.0, ALU.add, ALU.max
                                        ).then_inc(dve_out, 1)

            def four_tiles(t, first=False, last=False):
                lay_over(t, 0, 0)
                if not first:
                    tower(t - 1, 1)
                keep_turned(t, 1)
                lay_over(t, 0, 1)
                lay_over(t, 1, 0)
                if not first:
                    keep_turned(t, 2)
                if not last:
                    one_hots(t + 1, 0, range(4))
                lay_over(t, 1, 1)
                if not last:
                    one_hots(t + 1, 0, range(4, OH_CHUNKS))
                move_slots(t, 0)
                if not last:
                    for k in range(1, NO):
                        one_hots(t + 1, k)
                        if first and k == NO // 2:
                            keep_turned(t, 2)
                lay_over(t, 2, 0)
                if last:
                    tower(t, 0)
                keep_turned(t, 3)
                lay_over(t, 2, 1)
                if not last:
                    tower(t, 0)
                lay_over(t, 3, 0)
                if not last:
                    keep_turned(t + 1, 0)
                lay_over(t, 3, 1)
                move_slots(t, 1)
                if last:
                    tower(t, 1)

            dve.wait_ge(row_numbers_loaded, 16)
            one_hots(0, 0, range(4))
            split_low(0)
            one_hots(0, 0, range(4, OH_CHUNKS))
            for k in range(1, NO):
                split_low(k)
                if k == NO - 1:
                    keep_turned(0, 0)
                one_hots(0, k)
            dve.wait_ge(weights_loaded, 16 * N_WEIGHTS)
            dve.wait_ge(consts_loaded, 16 * N_CONSTS)
            nc.vector.tensor_tensor(w1d[:], w1d[:], w1d_last[:], ALU.add).then_inc(w1d_summed, 1)
            four_tiles(0, first=True)
            with dve.Fori(1, NB - 1) as t:
                four_tiles(t)
            four_tiles(NB - 1, last=True)


def kernel(**inputs):
    import concourse.bacc as _bacc
    from concourse.bass_utils import run_bass_kernel_spmd as _run

    a = {k: np.ascontiguousarray(v) for k, v in inputs.items()}
    w = a["W_top1"]
    w1_pairs = np.zeros((KCH, 128, H1), w.dtype)
    over_mask = np.zeros((128, NSLOT - 1), np.int32)
    for slot in range(NSLOT):
        for row in range(NF):
            position, over = slot_source(row, slot)
            if position is None:
                continue
            w1_pairs[slot % SPQ, QUAD * (slot // SPQ) + row] = w[top1_row(ORDER[row], ORDER[position])]
            if over:
                over_mask[row::QUAD, slot] = 1
    arrays = {
        "ids": a["ids"],
        "one_hot_ids": np.ascontiguousarray(a["ids"][:, ONE_HOT].T)[None],
        "x_t": np.ascontiguousarray(a["r_dense_features"].T),
        "w1_pairs": w1_pairs,
        "w_top1": w,
        "b1_cols": np.ascontiguousarray(a["b_top1"].reshape(-1, 128).T),
        "w_top2": a["W_top2"],
        "b2_cols": np.ascontiguousarray(a["b_top2"].reshape(-1, 128).T),
        "w3_cols": np.ascontiguousarray(a["W_top3"].reshape(-1, 128).T),
        "row_numbers": np.arange(128 * OH_CHUNKS, dtype=np.float32).reshape(128, OH_CHUNKS),
        "over_mask": over_mask,
        "identity": np.eye(128, dtype=np.float32),
    }
    tables = {f"tbl_{f}": a[f"tbl_{f}"] for f in range(F)}

    nc = _bacc.Bacc("TRN2", target_bir_lowering=False, num_devices=1)

    def dram(name, array):
        return nc.dram_tensor(f"in_{name}", array.shape, mybir.dt.from_np(array.dtype), kind="ExternalInput").ap()

    args = {name: dram(name, array) for name, array in arrays.items()}
    args["tables"] = [dram(name, array) for name, array in tables.items()]
    args["out"] = nc.dram_tensor("out", (1, B), F32, kind="ExternalOutput").ap()
    build(nc, **args)
    r = _run(nc, [{f"in_{name}": array for name, array in (arrays | tables).items()}], core_ids=[0])
    return r.results[0]["out"].reshape(B, 1)
```

```python
from contextlib import ExitStack

import concourse.bass as bass
import numpy as np
from concourse import mybir

ALU = mybir.AluOpType
ACT = mybir.ActivationFunctionType
F32 = mybir.dt.float32
F32R = mybir.dt.float32r
I32 = mybir.dt.int32

B, F, D = 2048, 26, 128
H1, H2 = 512, 256
NF = F + 1
TILE = 128
PAIR = 2 * TILE
SET = 4 * TILE
NT, NP, NB = B // TILE, B // PAIR, B // SET

ONE_HOT = (2, 12, 17, 18, 19, 20, 24, 25)
GATHERED = tuple(f for f in range(F) if f not in ONE_HOT)
NO, NG = len(ONE_HOT), len(GATHERED)
OH_ROWS = 1000
OH_CHUNKS = 8
OH_K = OH_ROWS // OH_CHUNKS
N_IDS = NO // 2
N_STAGED = 4
ORDER = GATHERED + ONE_HOT + (F,)

HALF = NF // 2
NSLOT = HALF + 1
LABEL = [(-s) % NF for s in range(NSLOT)] + [(HALF - s) % NF for s in range(NSLOT - 1)]
QUAD = 32
SPQ = 4
KCH = SPQ


def slot_source(row, slot):
    for over, position in ((False, slot), (True, NSLOT + slot)):
        if position < NF and 1 <= (LABEL[position] - LABEL[row]) % NF <= HALF:
            return position, over
    return None, False


def top1_row(a, b):
    a, b = min(a, b), max(a, b)
    if b == F:
        return D + a
    return D + F + a * F - a * (a + 1) // 2 + (b - a - 1)


def build(nc, gather_ids, one_hot_ids, x_t, tables, w1_pairs, w_top1, b1_cols, w_top2, b2_cols, w3_cols,
          row_numbers, over_mask, identity, out):
    with ExitStack() as ctx:
        def sb(name, shape, dt, stack=ctx):
            return stack.enter_context(nc.sbuf_tensor(name, shape, dt))

        def sem(name):
            return ctx.enter_context(nc.semaphore(name))

        index_all = sb("index_all", [128, NT, NG], I32)
        index_now = sb("index_now", [128, 4, NG], I32)
        gathered = sb("gathered", [128, 4, NG, D], F32)
        fixed = sb("fixed", [128, NO, SET], F32)
        dense_t = sb("dense_t", [128, B], F32)
        high = [sb(f"high{k}", [OH_K, OH_CHUNKS, D], F32R) for k in range(NO)]
        low = [sb(f"low{k}", [OH_K, OH_CHUNKS, D], F32R) for k in range(NO)]
        ids_row = sb("ids_row", [128, N_IDS, SET], I32)
        onehot = [sb(f"onehot{i}", [OH_K, SET], F32R) for i in range(4)]
        embed = [sb(f"embed{i}", [128, TILE, NF], F32) for i in range(2)]
        w1p = sb("w1p", [128, KCH, H1], F32)
        w1d = sb("w1d", [128, H1], F32)
        w2 = sb("w2", [128, H1 // 128, H2], F32)
        w3 = sb("w3", [128, H2 // 128], F32)
        b1 = sb("b1", [128, H1 // 128], F32)
        b2 = sb("b2", [128, H2 // 128], F32)
        row_no = sb("row_no", [128, OH_CHUNKS], F32)
        mask = sb("mask", [128, NSLOT - 1], I32)
        ident = sb("ident", [128, 128], F32)

        with ExitStack() as preparation:
            table = [sb(f"table{i}", [OH_K, OH_CHUNKS, D], F32, preparation) for i in range(N_STAGED)]
            w1d_last = sb("w1d_last", [128, H1], F32, preparation)

        slots = sb("slots", [128, NSLOT, 64], F32)
        zpairs = [sb(f"zpairs{i}", [128, KCH, PAIR], F32) for i in range(2)]
        h1 = sb("h1", [128, H1 // 128, PAIR], F32)
        h2 = sb("h2", [128, H2 // 128, PAIR], F32)

        turned = [ctx.enter_context(nc.psum_tensor(f"turned{i}", [128, 4, 128], F32)) for i in range(2)]
        gram = [ctx.enter_context(nc.psum_tensor(f"gram{i}", [128, 512], F32)) for i in range(2)]
        acc = ctx.enter_context(nc.psum_tensor("acc", [128, 4, 512], F32))

        index_loaded = sem("index_loaded")
        row_numbers_loaded = sem("row_numbers_loaded")
        consts_loaded = sem("consts_loaded")
        weights_loaded = sem("weights_loaded")
        dense_loaded = sem("dense_loaded")
        first_ids_loaded = [sem(f"first_ids_loaded{i}") for i in range(N_IDS)]
        ids_loaded = sem("ids_loaded")
        late_ids_loaded = [sem(f"late_ids_loaded{i}") for i in range(N_IDS)]
        table_loaded = [sem(f"table_loaded{i}") for i in range(N_STAGED)]
        high_ready = sem("high_ready")
        low_ready = sem("low_ready")
        onehot_ready = sem("onehot_ready")
        onehot_used = sem("onehot_used")
        lookup_ready = sem("lookup_ready")
        lookup_kept = sem("lookup_kept")
        index_ready = sem("index_ready")
        rows_landed = [sem(f"rows_landed{i}") for i in range(4)]
        turned_ready = [sem(f"turned_ready{i}") for i in range(2)]
        turned_kept = [sem(f"turned_kept{i}") for i in range(2)]
        fixed_placed = sem("fixed_placed")
        gram_ready = sem("gram_ready")
        slots_copied = sem("slots_copied")
        slots_ready = sem("slots_ready")
        w1d_summed = sem("w1d_summed")
        moved_act = sem("moved_act")
        moved_dve = sem("moved_dve")
        act_in = sem("act_in")
        act_out = sem("act_out")
        dve_in = sem("dve_in")
        dve_out = sem("dve_out")
        y_stored = sem("y_stored")

        N_CONSTS, N_WEIGHTS = 2, 7

        block = ctx.enter_context(nc.Block())

        GROUPS = [range(g, min(g + 4, NG)) for g in range(0, NG, 4)]
        NGR = len(GROUPS)
        assert NGR % 2 == 1

        def groups_before(t, m, g, parity):
            return (2 * NGR) * t + (NGR * m + g + (1 - parity)) // 2

        USED = OH_CHUNKS - 1

        TURNING = 4

        MOVED_BY_ACT = (3, 2)

        def due(value):
            return not isinstance(value, int) or value > 0

        @block.sync
        def _(sp):
            sp.dma_start(index_all[:], gather_ids.rearrange("(n p) g -> p n g", p=128)).then_inc(index_loaded, 16)
            sp.dma_start(row_no[:], row_numbers).then_inc(row_numbers_loaded, 16)
            for k in range(NO):
                if k < N_IDS:
                    sp.dma_start(ids_row[:, k, :], one_hot_ids[:, k, 0:SET].to_broadcast([128, SET])
                                 ).then_inc(first_ids_loaded[k], 16)
                if k >= N_STAGED:
                    sp.wait_ge(low_ready, k - N_STAGED + 1)
                sp.dma_start(table[k % N_STAGED][:], tables[ONE_HOT[k]].rearrange("(p c) d -> p c d", c=OH_CHUNKS)
                             ).then_inc(table_loaded[k % N_STAGED], 16)
            sp.dma_start(ident[:], identity).then_inc(consts_loaded, 16)
            sp.dma_start(mask[:], over_mask).then_inc(consts_loaded, 16)
            sp.dma_start(dense_t[:], x_t).then_inc(dense_loaded, 16)
            sp.dma_start(w1d[:], w_top1[0:D, :]).then_inc(weights_loaded, 16)
            sp.dma_start(w1d_last[:], w_top1[w_top1.shape[0] - D:w_top1.shape[0], :]).then_inc(weights_loaded, 16)
            sp.dma_start(b1[:], b1_cols).then_inc(weights_loaded, 16)
            sp.dma_start(w1p[:], w1_pairs.rearrange("c p h -> p c h")).then_inc(weights_loaded, 16)
            sp.dma_start(w2[:], w_top2.rearrange("(k p) h -> p k h", p=128)).then_inc(weights_loaded, 16)
            sp.dma_start(b2[:], b2_cols).then_inc(weights_loaded, 16)
            sp.dma_start(w3[:], w3_cols).then_inc(weights_loaded, 16)

            sp.wait_ge(act_out, 4 * NP)
            sp.dma_start(out, dense_t[0:1, :]).then_inc(y_stored, 16)
            sp.wait_ge(y_stored, 16)

        @block.gpsimd
        def _(pool):
            pool.wait_ge(index_loaded, 16)

            def copy_index(t, m):
                nc.gpsimd.tensor_copy(index_now[:, m, :], index_all[:, 4 * t + m, :]).then_inc(index_ready, 1)

            def gather(t, m, last=False):
                pool.wait_ge(index_ready, 4 * t + m + 1)
                end = (NGR * m + NGR - 1) % 2
                if due(groups_before(t - 1, m, NGR, end)):
                    pool.wait_ge(turned_ready[end], groups_before(t - 1, m, NGR, end))
                tn, mn = (t, m + 1) if m < 3 else (t + 1, 0)
                if due(tn):
                    pool.wait_ge(rows_landed[mn], 16 * NG * tn)
                if not last:
                    copy_index(tn, mn)
                for g, f in enumerate(GATHERED):
                    nc.gpsimd.indirect_dma_start(
                        gathered[:, m, g, :], None, tables[f],
                        bass.IndirectOffsetOnAxis(ap=index_now[:, m, g:g + 1], axis=0),
                    ).then_inc(rows_landed[m], 16)

            copy_index(0, 0)
            for m in range(4):
                gather(0, m)
            with pool.Fori(1, NB - 1) as t:
                for m in range(4):
                    gather(t, m)
            for m in range(4):
                gather(NB - 1, m, last=(m == 3))

        @block.tensor
        def _(pe):
            def look_up(t, k, turning=None):
                q = NO * t + k
                if due(q - 1):
                    pe.wait_ge(lookup_kept, q - 1)
                if isinstance(t, int) and t == 0:
                    pe.wait_ge(high_ready, k + 1)
                    pe.wait_ge(low_ready, k + 1)
                for c in range(OH_CHUNKS):
                    if turning and c - 1 in range(NGR):
                        transpose_rows(*turning, groups=[c - 1])
                    pe.wait_ge(onehot_ready, OH_CHUNKS * q + c + 1)
                    nc.tensor.matmul(acc[:, k % 2, :], high[k][:, c, :], onehot[c % 4][:],
                                     start=(c == 0), stop=False)
                    nc.tensor.matmul(acc[:, k % 2, :], low[k][:, c, :], onehot[c % 4][:],
                                     start=False, stop=(c == USED)
                                     ).then_inc(onehot_used if c < USED else lookup_ready, 1)

            def transpose_rows(t, m, groups=range(NGR)):
                for g in groups:
                    if g == 0:
                        pe.wait_ge(rows_landed[m], 16 * NG * (t + 1))
                    parity = (NGR * m + g) % 2
                    if due(groups_before(t, m, g, parity)):
                        pe.wait_ge(turned_kept[parity], groups_before(t, m, g, parity))
                    for n, r in enumerate(GROUPS[g]):
                        mm = nc.tensor.transpose(turned[parity][:, n, :], gathered[:, m, r, :], ident[:])
                    mm.then_inc(turned_ready[parity], 1)

            def gram_half(t, m, b, turning=None):
                if b == 0:
                    pe.wait_ge(fixed_placed, 4 * t + m + 1)
                    pe.wait_ge(turned_kept[0], groups_before(t, m, NGR, 0))
                    pe.wait_ge(turned_kept[1], groups_before(t, m, NGR, 1))
                if due(8 * t + 2 * m + b - 1):
                    pe.wait_ge(slots_ready, 8 * t + 2 * m + b - 1)
                for i in range(16):
                    if turning and i % 2 == 0 and i // 2 - 1 in range(NGR):
                        transpose_rows(*turning, groups=[i // 2 - 1])
                    for j in range(4):
                        rows = embed[m % 2][:, 32 * j + 16 * b + i, :]
                        mm = nc.tensor.matmul(gram[b][QUAD * j:QUAD * j + NF, NF * i:NF * (i + 1)],
                                              rows, rows, start=True, stop=True)
                mm.then_inc(gram_ready, 1)

            def first_layer(t, a, last=False):
                u = 2 * t + a
                dense = dense_t[:, bass.ds(PAIR * u, PAIR)].rearrange("p (n j i) -> p j n i", n=2, j=4)

                def dense_product(c):
                    nc.tensor.matmul(acc[:, c % 2, 0:PAIR], w1d[:, 128 * c:128 * (c + 1)], dense,
                                     start=True, stop=False)

                if a == 0 and not last:
                    pe.wait_ge(lookup_kept, NO * (t + 2))
                dense_product(0)
                dense_product(1)
                pe.wait_ge(moved_act, u + 1)
                pe.wait_ge(moved_dve, u + 1)
                for c in range(4):
                    cols = slice(128 * c, 128 * (c + 1))
                    if c == 2:
                        pe.wait_ge(act_out, 4 * u + 1)
                        dense_product(c)
                    if c == 3:
                        pe.wait_ge(dve_out, 3 * u + 1)
                        dense_product(c)
                    for s in range(KCH):
                        k = QUAD * sum(SPQ * q + s < NSLOT for q in range(4))
                        mm = nc.tensor.matmul(acc[:, c % 2, 0:PAIR], w1p[0:k, s, cols], zpairs[a][0:k, s, :],
                                              start=False, stop=(s == KCH - 1))
                    mm.then_inc(act_in if c % 2 == 0 else dve_in, 1)

            def second_layer(t, a):
                u = 2 * t + a
                for c in range(4):
                    if c % 2 == 0:
                        pe.wait_ge(act_out, 4 * u + 1 + c // 2)
                    else:
                        pe.wait_ge(dve_out, 3 * u + 1 + c // 2)
                    for o in range(2):
                        mm = nc.tensor.matmul(acc[:, 2 + o, 0:PAIR], w2[:, c, 128 * o:128 * (o + 1)], h1[:, c, :],
                                              start=(c == 0), stop=(c == 3))
                        if c == 3:
                            mm.then_inc(act_in if o == 0 else dve_in, 1)

            def third_layer(t, a):
                u = 2 * t + a
                for c in range(2):
                    if c == 0:
                        pe.wait_ge(act_out, 4 * u + 3)
                    else:
                        pe.wait_ge(dve_out, 3 * u + 3)
                    for j in range(4):
                        mm = nc.tensor.matmul(acc[QUAD * j:QUAD * j + 1, 2, 64 * j:64 * (j + 1)], w3[:, c:c + 1],
                                              h2[:, c, 64 * j:64 * (j + 1)], start=(c == 0), stop=(c == 1))
                mm.then_inc(act_in, 1)

            def tower(t, a):
                first_layer(t, a)
                second_layer(t, a)

            def four_tiles(t, first=False, last=False):
                gram_half(t, 0, 0)
                if not first and not last:
                    tower(t - 1, 1)
                gram_half(t, 0, 1, turning=(t, 1))
                if not first and not last:
                    third_layer(t - 1, 1)
                gram_half(t, 1, 0)
                if last:
                    first_layer(t - 1, 1, last)
                gram_half(t, 1, 1, turning=(t, 2) if last else None)
                if not last:
                    for k in range(NO):
                        look_up(t + 1, k, turning=(t, 2) if k == TURNING else None)
                gram_half(t, 2, 0)
                if last:
                    second_layer(t - 1, 1)
                    third_layer(t - 1, 1)
                    first_layer(t, 0, last)
                gram_half(t, 2, 1, turning=(t, 3))
                if first:
                    pe.wait_ge(weights_loaded, 16 * N_WEIGHTS)
                    pe.wait_ge(w1d_summed, 1)
                if not last:
                    tower(t, 0)
                gram_half(t, 3, 0)
                if not last:
                    third_layer(t, 0)
                gram_half(t, 3, 1, turning=None if last else (t + 1, 0))
                if last:
                    second_layer(t, 0)
                    third_layer(t, 0)
                    tower(t, 1)
                    third_layer(t, 1)

            for k in range(NO):
                if k == NO - 1:
                    pe.wait_ge(consts_loaded, 16 * N_CONSTS)
                look_up(0, k, turning=(0, 0) if k == NO - 1 else None)
            four_tiles(0, first=True)
            with pe.Fori(1, NB - 1) as t:
                four_tiles(t)
            four_tiles(NB - 1, last=True)

        @block.scalar
        def _(act):
            def split_high(k):
                act.wait_ge(table_loaded[k % N_STAGED], 16 * (k // N_STAGED + 1))
                nc.scalar.copy(high[k][:], table[k % N_STAGED][:]).then_inc(high_ready, 1)

            def keep_lookup(t, k):
                act.wait_ge(lookup_ready, NO * t + k + 1)
                nc.scalar.copy(fixed[:, k, :], acc[:, k % 2, :]).then_inc(lookup_kept, 1)
                if k + N_IDS < NO:
                    act.dma_start(ids_row[:, k, :],
                                  one_hot_ids[:, k + N_IDS, bass.ds(SET * t, SET)].to_broadcast([128, SET])
                                  ).then_inc(late_ids_loaded[k], 16)

            def load_ids(t):
                act.dma_start(ids_row[:],
                              one_hot_ids[:, 0:N_IDS, bass.ds(SET * t, SET)].to_broadcast([128, N_IDS, SET])
                              ).then_inc(ids_loaded, 16)

            def keep_turned(t, m):
                if due(8 * t + 2 * m - 2):
                    act.wait_ge(gram_ready, 8 * t + 2 * m - 2)
                for g, group in enumerate(GROUPS):
                    if (NGR * m + g) % 2 == 0:
                        act.wait_ge(turned_ready[0], groups_before(t, m, g, 0) + 1)
                        nc.scalar.copy(embed[m % 2][:, :, group[0]:group[-1] + 1].rearrange("p n f -> p f n"),
                                       turned[0][:, 0:len(group), :]).then_inc(turned_kept[0], 1)

            def place_fixed(t, m, part=0):
                if due(8 * t + 2 * m - 2):
                    act.wait_ge(gram_ready, 8 * t + 2 * m - 2)
                if part != 2:
                    nc.scalar.copy(embed[m % 2][:, :, F], dense_t[:, bass.ds(TILE * (4 * t + m), TILE)])
                r = F - 1 if part == 2 else NG
                end = F - 1 if part == 1 else F
                ins = nc.scalar.copy(embed[m % 2][:, :, r:end].rearrange("p n f -> p f n"),
                                     fixed[:, r - NG:end - NG, TILE * m:TILE * (m + 1)])
                if part != 1:
                    ins.then_inc(fixed_placed, 1)

            def copy_slots(t, m, b):
                if m % 2 == 0 and b == 0 and due(2 * t + m // 2):
                    act.wait_ge(moved_act, 2 * t + m // 2)
                    act.wait_ge(moved_dve, 2 * t + m // 2)
                act.wait_ge(gram_ready, 8 * t + 2 * m + b + 1)
                i0 = 32 * (m % 2) + 16 * b
                nc.scalar.copy(slots[:, 0:NSLOT - 1, i0:i0 + 16],
                               gram[b][:, 0:16 * NF].rearrange("p (i f) -> p f i", f=NF)[:, 0:NSLOT - 1, :]
                               ).then_inc(slots_copied, 1)

            def move_slots(t, a):
                act.wait_ge(slots_ready, 8 * t + 4 * (a + 1))
                for j in range(MOVED_BY_ACT[a]):
                    for q in range(4):
                        n = min(SPQ, NSLOT - SPQ * q)
                        ins = nc.scalar.copy(zpairs[a][QUAD * q:QUAD * (q + 1), 0:n, 64 * j:64 * (j + 1)],
                                             slots[QUAD * j:QUAD * (j + 1), SPQ * q:SPQ * q + n, :])
                ins.then_inc(moved_act, 1)

            def first_layer(t, a):
                u = 2 * t + a
                for n, c in enumerate((0, 2)):
                    act.wait_ge(act_in, 4 * u + n + 1)
                    nc.scalar.activation(h1[:, c, :], acc[:, 0, 0:PAIR], ACT.Relu, bias=b1[:, c:c + 1]
                                         ).then_inc(act_out, 1)

            def second_layer(t, a):
                u = 2 * t + a
                act.wait_ge(act_in, 4 * u + 3)
                nc.scalar.activation(h2[:, 0, :], acc[:, 2, 0:PAIR], ACT.Relu, bias=b2[:, 0:1]).then_inc(act_out, 1)

            def third_layer(t, a):
                u = 2 * t + a
                act.wait_ge(act_in, 4 * u + 4)
                y = dense_t[0:1, bass.ds(PAIR * u, PAIR)].rearrange("p (n j i) -> p j n i", n=2, j=4)
                for j in range(4):
                    ins = nc.scalar.copy(y[:, j], acc[QUAD * j:QUAD * j + 1, 2, 64 * j:64 * (j + 1)].rearrange(
                        "p (n i) -> p n i", n=2))
                ins.then_inc(act_out, 1)

            def tower(t, a):
                first_layer(t, a)
                second_layer(t, a)

            def four_tiles(t, first=False, last=False):
                if not last and not first:
                    load_ids(t + 1)
                copy_slots(t, 0, 0)
                place_fixed(t, 1)
                if not first and not last:
                    tower(t - 1, 1)
                keep_turned(t, 1)
                copy_slots(t, 0, 1)
                if not first and not last:
                    third_layer(t - 1, 1)
                copy_slots(t, 1, 0)
                place_fixed(t, 2)
                if last:
                    first_layer(t - 1, 1)
                    keep_turned(t, 2)
                copy_slots(t, 1, 1)
                if not last:
                    place_fixed(t, 3)
                    act.wait_ge(fixed_placed, 4 * t + 4)
                    for k in range(NO):
                        if k == TURNING:
                            keep_turned(t, 2)
                        keep_lookup(t + 1, k)
                        if k == 0:
                            move_slots(t, 0)
                else:
                    move_slots(t, 0)
                copy_slots(t, 2, 0)
                if last:
                    second_layer(t - 1, 1)
                    third_layer(t - 1, 1)
                    first_layer(t, 0)
                    place_fixed(t, 3)
                keep_turned(t, 3)
                copy_slots(t, 2, 1)
                if not last:
                    tower(t, 0)
                copy_slots(t, 3, 0)
                if not last:
                    third_layer(t, 0)
                    act.wait_ge(lookup_kept, NO * (t + 2))
                    place_fixed(t + 1, 0)
                    keep_turned(t + 1, 0)
                copy_slots(t, 3, 1)
                move_slots(t, 1)
                if last:
                    second_layer(t, 0)
                    third_layer(t, 0)
                    tower(t, 1)
                    third_layer(t, 1)

            split_high(0)
            split_high(1)
            for k in range(NO):
                if k + 2 < NO:
                    split_high(k + 2)
                if k == NO - 1:
                    keep_turned(0, 0)
                    act.wait_ge(dense_loaded, 16)
                    act.wait_ge(lookup_kept, NO - 1)
                    place_fixed(0, 0, part=1)
                keep_lookup(0, k)
            act.wait_ge(lookup_kept, NO)
            place_fixed(0, 0, part=2)
            load_ids(1)
            act.wait_ge(weights_loaded, 16 * N_WEIGHTS)
            four_tiles(0, first=True)
            with act.Fori(1, NB - 1) as t:
                four_tiles(t)
            four_tiles(NB - 1, last=True)

        @block.vector
        def _(dve):
            for b in range(2):
                nc.vector.memset(gram[b][:], 0.0)

            def split_low(k):
                dve.wait_ge(table_loaded[k % N_STAGED], 16 * (k // N_STAGED + 1))
                dve.wait_ge(high_ready, k + 1)
                nc.vector.tensor_tensor(low[k][:], table[k % N_STAGED][:], high[k][:].bitcast(F32), ALU.subtract
                                        ).then_inc(low_ready, 1)

            def one_hots(t, k, chunks=range(OH_CHUNKS), turning=None):
                q = NO * t + k
                for c in chunks:
                    if turning and c >= 4:
                        keep_turned(*turning, groups=[c - 4] if c < USED else range(c - 4, NGR))
                    if c == 0:
                        if k >= N_IDS:
                            dve.wait_ge(late_ids_loaded[k - N_IDS], 16 * (t + 1))
                        elif isinstance(t, int) and t == 0:
                            dve.wait_ge(first_ids_loaded[k], 16)
                        else:
                            dve.wait_ge(ids_loaded, 16 * t)
                    if c >= 4:
                        dve.wait_ge(onehot_used, USED * q + c - 3)
                    elif due(q):
                        if c == 3:
                            dve.wait_ge(lookup_ready, q)
                        else:
                            dve.wait_ge(onehot_used, USED * (q - 1) + c + 5)
                    nc.vector.tensor_scalar(onehot[c % 4][:], ids_row[0:OH_K, k % N_IDS, :],
                                            row_no[0:OH_K, c:c + 1], None, ALU.is_equal
                                            ).then_inc(onehot_ready, 1)

            def keep_turned(t, m, groups=range(NGR)):
                if 0 in groups and due(8 * t + 2 * m - 2):
                    dve.wait_ge(gram_ready, 8 * t + 2 * m - 2)
                for g in groups:
                    group = GROUPS[g]
                    if (NGR * m + g) % 2 == 1:
                        dve.wait_ge(turned_ready[1], groups_before(t, m, g, 1) + 1)
                        nc.vector.tensor_copy(embed[m % 2][:, :, group[0]:group[-1] + 1].rearrange("p n f -> p f n"),
                                              turned[1][:, 0:len(group), :]).then_inc(turned_kept[1], 1)

            def lay_over(t, m, b):
                dve.wait_ge(slots_copied, 8 * t + 2 * m + b + 1)
                i0 = 32 * (m % 2) + 16 * b
                columns = gram[b][:, 0:16 * NF].rearrange("p (i f) -> p f i", f=NF)
                nc.vector.tensor_copy(slots[:, NSLOT - 1, i0:i0 + 16], columns[:, NSLOT - 1, :])
                nc.vector.copy_predicated(
                    slots[:, 0:NSLOT - 1, i0:i0 + 16],
                    mask[:].unsqueeze(2).to_broadcast([128, NSLOT - 1, 16]), columns[:, NSLOT:NF, :]
                ).then_inc(slots_ready, 1)

            def move_slots(t, a):
                dve.wait_ge(slots_ready, 8 * t + 4 * (a + 1))
                for j in range(MOVED_BY_ACT[a], 4):
                    for q in range(4):
                        n = min(SPQ, NSLOT - SPQ * q)
                        ins = nc.vector.tensor_copy(zpairs[a][QUAD * q:QUAD * (q + 1), 0:n, 64 * j:64 * (j + 1)],
                                                    slots[QUAD * j:QUAD * (j + 1), SPQ * q:SPQ * q + n, :])
                ins.then_inc(moved_dve, 1)

            def first_layer(t, a):
                u = 2 * t + a
                for n, c in enumerate((1, 3)):
                    dve.wait_ge(dve_in, 3 * u + n + 1)
                    nc.vector.tensor_scalar(h1[:, c, :], acc[:, 1, 0:PAIR], b1[:, c:c + 1], 0.0, ALU.add, ALU.max
                                            ).then_inc(dve_out, 1)

            def second_layer(t, a):
                u = 2 * t + a
                dve.wait_ge(dve_in, 3 * u + 3)
                nc.vector.tensor_scalar(h2[:, 1, :], acc[:, 3, 0:PAIR], b2[:, 1:2], 0.0, ALU.add, ALU.max
                                        ).then_inc(dve_out, 1)

            def tower(t, a):
                first_layer(t, a)
                second_layer(t, a)

            def four_tiles(t, first=False, last=False):
                lay_over(t, 0, 0)
                if not first and not last:
                    tower(t - 1, 1)
                keep_turned(t, 1)
                lay_over(t, 0, 1)
                lay_over(t, 1, 0)
                if last:
                    first_layer(t - 1, 1)
                    keep_turned(t, 2)
                if not last:
                    one_hots(t + 1, 0, range(4))
                lay_over(t, 1, 1)
                if not last:
                    one_hots(t + 1, 0, range(4, OH_CHUNKS))
                move_slots(t, 0)
                if not last:
                    for k in range(1, NO):
                        one_hots(t + 1, k, turning=(t, 2) if k == TURNING else None)
                lay_over(t, 2, 0)
                if last:
                    second_layer(t - 1, 1)
                    first_layer(t, 0)
                keep_turned(t, 3)
                lay_over(t, 2, 1)
                if not last:
                    tower(t, 0)
                lay_over(t, 3, 0)
                if not last:
                    keep_turned(t + 1, 0)
                lay_over(t, 3, 1)
                move_slots(t, 1)
                if last:
                    second_layer(t, 0)
                    tower(t, 1)

            dve.wait_ge(row_numbers_loaded, 16)
            one_hots(0, 0, range(4))
            split_low(0)
            one_hots(0, 0, range(4, OH_CHUNKS))
            for k in range(1, NO):
                split_low(k)
                one_hots(0, k, turning=(0, 0) if k == NO - 1 else None)
            dve.wait_ge(consts_loaded, 16 * N_CONSTS)
            dve.wait_ge(weights_loaded, 16 * N_WEIGHTS)
            nc.vector.tensor_tensor(w1d[:], w1d[:], w1d_last[:], ALU.add).then_inc(w1d_summed, 1)
            four_tiles(0, first=True)
            with dve.Fori(1, NB - 1) as t:
                four_tiles(t)
            four_tiles(NB - 1, last=True)


def kernel(**inputs):
    import concourse.bacc as _bacc
    from concourse.bass_utils import run_bass_kernel_spmd as _run

    a = {k: np.ascontiguousarray(v) for k, v in inputs.items()}
    w = a["W_top1"]
    w1_pairs = np.zeros((KCH, 128, H1), w.dtype)
    over_mask = np.zeros((128, NSLOT - 1), np.int32)
    for slot in range(NSLOT):
        for row in range(NF):
            position, over = slot_source(row, slot)
            if position is None:
                continue
            w1_pairs[slot % SPQ, QUAD * (slot // SPQ) + row] = w[top1_row(ORDER[row], ORDER[position])]
            if over:
                over_mask[row::QUAD, slot] = 1
    arrays = {
        "gather_ids": np.ascontiguousarray(a["ids"][:, GATHERED]),
        "one_hot_ids": np.ascontiguousarray(a["ids"][:, ONE_HOT].T)[None],
        "x_t": np.ascontiguousarray(a["r_dense_features"].T),
        "w1_pairs": w1_pairs,
        "w_top1": w,
        "b1_cols": np.ascontiguousarray(a["b_top1"].reshape(-1, 128).T),
        "w_top2": a["W_top2"],
        "b2_cols": np.ascontiguousarray(a["b_top2"].reshape(-1, 128).T),
        "w3_cols": np.ascontiguousarray(a["W_top3"].reshape(-1, 128).T),
        "row_numbers": np.arange(128 * OH_CHUNKS, dtype=np.float32).reshape(128, OH_CHUNKS),
        "over_mask": over_mask,
        "identity": np.eye(128, dtype=np.float32),
    }
    tables = {f"tbl_{f}": a[f"tbl_{f}"] for f in range(F)}

    nc = _bacc.Bacc("TRN2", target_bir_lowering=False, num_devices=1)

    def dram(name, array):
        return nc.dram_tensor(f"in_{name}", array.shape, mybir.dt.from_np(array.dtype), kind="ExternalInput").ap()

    args = {name: dram(name, array) for name, array in arrays.items()}
    args["tables"] = [dram(name, array) for name, array in tables.items()]
    args["out"] = nc.dram_tensor("out", (1, B), F32, kind="ExternalOutput").ap()
    build(nc, **args)
    r = _run(nc, [{f"in_{name}": array for name, array in (arrays | tables).items()}], core_ids=[0])
    return r.results[0]["out"].reshape(B, 1)
```
